# Optimizing a Trainium2 kernel written in Bass

```python
import numpy as np
import jax
import jax.numpy as jnp

def _softmax(x, axis=-1):
    return jax.nn.softmax(x, axis=axis)

def _gelu(x):
    return jax.nn.gelu(x, approximate=True)

def _silu(x):
    return jax.nn.silu(x)

def _sigmoid(x):
    return jax.nn.sigmoid(x)

def _layernorm(x, axis=-1, eps=1e-05):
    m = jnp.mean(x, axis=axis, keepdims=True)
    v = jnp.var(x, axis=axis, keepdims=True)
    return (x - m) / jnp.sqrt(v + eps)

def _scatter_add(tgt, idx, src, axis=0):
    return tgt.at[idx].add(src)

def _segment_sum(src, seg, n):
    return jax.ops.segment_sum(src, seg, n)
kernel_name = 'mk_cond_resid_d1_seqx_r2_f48a25'

def setup_inputs(seed: int=0):
    np.random.seed(seed)
    _w = jnp.asarray

    def _rec_inputs():
        import jax
        import jax.numpy as jnp
        _rk = jax.random.key(seed)
        x = -7.109e-05 + 0.9999 * jax.random.normal(jax.random.fold_in(_rk, 1), (128, 128, 512), jnp.float32)
        _lenS = 128 - jax.random.randint(jax.random.fold_in(_rk, 7), (128,), 0, max(1, 128 // 4) + 1, jnp.int32)
        _lenS2 = 128 - jax.random.randint(jax.random.fold_in(_rk, 8), (128,), 0, max(1, 128 // 4) + 1, jnp.int32)
        itok_B_0_8 = jax.random.randint(jax.random.fold_in(_rk, 11), (128,), 0, 9, jnp.int32)
        return (x, itok_B_0_8)
    x, itok_B_0_8 = _rec_inputs()

    def _L0_cond_setup():
        import jax, jax.numpy as jnp
        import numpy as np
        LN_EPS = 1e-05
        key = jax.random.key(seed)
        ks = jax.random.split(key, 8)
        B, S, H, A, L = (32, 1024, 512, 128, 10)
        return {'hidden_states': jax.random.normal(ks[0], (B, S, H), dtype=jnp.float32), 'language_ids': jax.random.randint(ks[1], (B,), 0, L, dtype=jnp.int64), 'W1': jax.random.normal(ks[2], (L, H, A), dtype=jnp.float32) * (1.0 / np.sqrt(H)), 'b1': jnp.zeros((L, A), dtype=jnp.float32), 'W2': jax.random.normal(ks[3], (L, A, H), dtype=jnp.float32) * (1.0 / np.sqrt(A)), 'b2': jnp.zeros((L, H), dtype=jnp.float32), 'gamma': jnp.ones((L, H), dtype=jnp.float32), 'beta': jnp.zeros((L, H), dtype=jnp.float32)}
    _L0_cond_all = _L0_cond_setup()
    _L0_cond_in = {k: v for k, v in _L0_cond_all.items() if k in ('W1', 'b1', 'W2', 'b2', 'gamma', 'beta')}
    del _L0_cond_all
    return {'x': x, 'itok_B_0_8': itok_B_0_8, 'L0_cond_W1': _L0_cond_in['W1'], 'L0_cond_b1': _L0_cond_in['b1'], 'L0_cond_W2': _L0_cond_in['W2'], 'L0_cond_b2': _L0_cond_in['b2'], 'L0_cond_gamma': _L0_cond_in['gamma'], 'L0_cond_beta': _L0_cond_in['beta']}

def reference(x, itok_B_0_8, L0_cond_W1, L0_cond_b1, L0_cond_W2, L0_cond_b2, L0_cond_gamma, L0_cond_beta):
    import jax
    import jax.numpy as jnp

    def _L0_cond_ref(hidden_states, language_ids, W1, b1, W2, b2, gamma, beta):
        import jax, jax.numpy as jnp
        import numpy as np
        LN_EPS = 1e-05
        w1 = W1[language_ids]
        w2 = W2[language_ids]
        h = jnp.einsum('bsh,bha->bsa', hidden_states, w1) + b1[language_ids][:, None, :]
        h = jax.nn.relu(h)
        adapted = jnp.einsum('bsa,bah->bsh', h, w2) + b2[language_ids][:, None, :]
        x = hidden_states + adapted
        mean = jnp.mean(x, axis=-1, keepdims=True)
        var = jnp.mean(jnp.square(x - mean), axis=-1, keepdims=True)
        normed = (x - mean) * jax.lax.rsqrt(var + LN_EPS)
        return normed * gamma[language_ids][:, None, :] + beta[language_ids][:, None, :]
    x = x + _L0_cond_ref(x, itok_B_0_8, L0_cond_W1, L0_cond_b1, L0_cond_W2, L0_cond_b2, L0_cond_gamma, L0_cond_beta)
    return x

_drawn_inputs = setup_inputs


def setup_inputs(seed=0):
    import zlib

    import numpy as np

    out = dict(_drawn_inputs(seed))
    spreads = {'L0_cond_b1': (0.0, 0.1),
     'L0_cond_b2': (0.0, 0.1),
     'L0_cond_gamma': (1.0, 0.2),
     'L0_cond_beta': (0.0, 0.1)}
    factors = {}
    for name, (base, spread) in spreads.items():
        noise = np.random.default_rng([zlib.crc32(name.encode()), seed]).standard_normal(out[name].shape)
        drawn = base * np.exp(spread * noise) if base else spread * noise
        out[name] = jnp.asarray(drawn.astype(out[name].dtype))
    for name, factor in factors.items():
        out[name] = (out[name] * factor).astype(out[name].dtype)
    return out
```

```python
from contextlib import ExitStack

import concourse.bass as bass
from concourse import mybir

F32 = mybir.dt.float32
BF16 = mybir.dt.bfloat16
I32 = mybir.dt.int32
ALU = mybir.AluOpType
ACT = mybir.ActivationFunctionType

LN_EPS = 1e-5
UNROLL = 8
PAIRS = UNROLL // 2
Y_BANKS = 4


def build(nc, x, ids, w1, b1, w2, b2, gamma, beta, out):
    B, S, H = x.shape
    L, _, A = w1.shape
    C = H // 128
    TURNS = B // UNROLL
    assert S == 128 and A == 128 and H == 512 and B % UNROLL == 0 and TURNS > 2

    x_pairs = x.rearrange("(n b) s h -> s n b h", b=2)
    out_pairs = out.rearrange("(n b) s h -> s n b h", b=2)

    with ExitStack() as ctx:
        def sb(name, shape, dt):
            return ctx.enter_context(nc.sbuf_tensor(name, shape, dt))

        def psum(name, shape, dt):
            return ctx.enter_context(nc.psum_tensor(name, shape, dt))

        def sem(name):
            return ctx.enter_context(nc.semaphore(name))

        w1_all = sb("w1_all", [128, L, C, A], F32)
        w2_all = sb("w2_all", [128, L, H], F32)
        gamma_all = sb("gamma_all", [128, L, H], F32)
        beta_all = sb("beta_all", [128, L, H], F32)
        b1_all = sb("b1_all", [128, L], F32)
        b2_parts = sb("b2_parts", [128, L, H], BF16)
        b2_rows = sb("b2_rows", [L, H], F32)
        b2_rest = sb("b2_rest", [L, 2, H], F32)
        b2_cut = sb("b2_cut", [L, 3, H], BF16)
        ones = sb("ones", [128, 128], BF16)
        identity = sb("identity", [128, 128], F32)
        ids_raw = sb("ids_raw", [1, B], I32)
        ids_fix = sb("ids_fix", [1, 2, B], F32)
        lang_ids = sb("lang_ids", [1, B], I32)
        eps = sb("eps", [128, 1], F32)
        x_in = sb("x_in", [128, UNROLL, H], F32)
        x_beta = sb("x_beta", [128, UNROLL, H], F32)
        x_T = sb("x_T", [128, 2, C, S], F32)
        w1_now = sb("w1_now", [128, 2, C, A], F32)
        h_T = sb("h_T", [128, 2, S], F32)
        y_out = sb("y_out", [128, UNROLL, H], F32)
        squares = sb("squares", [128, 2, H], F32)
        row_sum = sb("row_sum", [128, UNROLL], F32)
        mean = sb("mean", [128, UNROLL], F32)
        sq_sum = sb("sq_sum", [128, UNROLL], F32)
        std = sb("std", [128, UNROLL], F32)
        rstd = sb("rstd", [128, UNROLL], F32)

        ps_T = [psum(f"ps_T{i}", [128, C, S], F32) for i in range(2)]
        ps_h = [psum(f"ps_h{i}", [128, H], F32) for i in range(2)]
        ps_y = [psum(f"ps_y{i}", [128, H], F32) for i in range(Y_BANKS)]

        s_ids = sem("s_ids")
        s_b1 = sem("s_b1")
        s_b2 = sem("s_b2")
        s_w1 = sem("s_w1")
        s_w2 = sem("s_w2")
        s_gamma = sem("s_gamma")
        s_beta = sem("s_beta")
        x_loaded = [sem(f"x_loaded{i}") for i in range(PAIRS)]
        ids_step = sem("ids_step")
        ids_ready = sem("ids_ready")
        set_ready = sem("set_ready")
        identity_ready = sem("identity_ready")
        b2_step = sem("b2_step")
        b2_ready = sem("b2_ready")
        w1_staged = sem("w1_staged")
        x_beta_ready = sem("x_beta_ready")
        x_turned = sem("x_turned")
        x_T_ready = sem("x_T_ready")
        h_summed = sem("h_summed")
        h_T_ready = sem("h_T_ready")
        adapted = sem("adapted")
        y_ready = sem("y_ready")
        squared = sem("squared")
        scaled = sem("scaled")
        out_ready = sem("out_ready")
        mean_ready = sem("mean_ready")
        std_ready = sem("std_ready")
        rstd_ready = sem("rstd_ready")
        stored = [sem(f"stored{i}") for i in range(PAIRS)]

        block = ctx.enter_context(nc.Block())

        def lang_of(engine, t):
            return engine.value_load(lang_ids[0:1, bass.ds(t, 1)], min_val=0, max_val=L - 1)

        def of_lang(table, lang):
            return table[:, bass.ds(lang, 1), :].rearrange("p o h -> p (o h)")

        def all_turns(engine, turn):
            turn(0, True, False)
            with engine.Fori(1, TURNS - 1) as i:
                turn(i, False, False)
            turn(TURNS - 1, False, True)

        @block.sync
        def _(sp):
            sp.dma_start(ids_raw[:, :], ids.rearrange("(a b) -> a b", a=1)).then_inc(s_ids, 16)
            sp.dma_start(x_in[:, 0:2, :], x_pairs[:, 0, :, :]).then_inc(x_loaded[0], 16)
            sp.dma_start(w1_all[:, :, :, :], w1.rearrange("l (c p) a -> p l c a", p=128)).then_inc(s_w1, 16)
            sp.dma_start(w2_all[:, :, :], w2.rearrange("l a h -> a l h")).then_inc(s_w2, 16)
            sp.dma_start(x_in[:, 2:4, :], x_pairs[:, 1, :, :]).then_inc(x_loaded[1], 16)
            sp.dma_start(beta_all[:, :, :], beta.partition_broadcast(128)).then_inc(s_beta, 16)
            sp.dma_start(gamma_all[:, :, :], gamma.partition_broadcast(128)).then_inc(s_gamma, 16)
            for k in range(2, PAIRS):
                sp.dma_start(x_in[:, 2 * k:2 * k + 2, :], x_pairs[:, k, :, :]).then_inc(x_loaded[k], 16)

            def turn(i, first, last):
                for k in range(PAIRS):
                    done = i * UNROLL + 2 * k + 2
                    if not last:
                        sp.wait_ge(y_ready, done)
                        sp.wait_ge(x_beta_ready, done)
                        sp.dma_start(x_in[:, 2 * k:2 * k + 2, :],
                                     x_pairs[:, bass.ds((i + 1) * PAIRS + k, 1), :, :].rearrange("s o b h -> s (o b) h"))\
                            .then_inc(x_loaded[k], 16)
                    sp.wait_ge(out_ready, done)
                    sp.dma_start(out_pairs[:, bass.ds(i * PAIRS + k, 1), :, :].rearrange("s o b h -> s (o b) h"),
                                 y_out[:, 2 * k:2 * k + 2, :]).then_inc(stored[k], 16)

            all_turns(sp, turn)
            for k in range(PAIRS):
                sp.wait_ge(stored[k], 16 * TURNS)

        @block.gpsimd
        def _(pool):
            nc.gpsimd.memset(identity[:, :], 0.0).then_inc(set_ready, 1)
            nc.gpsimd.memset(ones[:, :], 1.0).then_inc(set_ready, 1)
            nc.gpsimd.memset(eps[:, :], LN_EPS).then_inc(set_ready, 1)
            nc.gpsimd.memset(b2_parts[:, :, :], 0.0).then_inc(set_ready, 1)
            pool.wait_ge(set_ready, 4)
            nc.gpsimd.affine_select(out=identity[:, :], in_=identity[:, :], compare_op=ALU.not_equal, fill=1.0,
                                    base=0, pattern=[[-1, 128]], channel_multiplier=1).then_inc(identity_ready, 1)
            pool.wait_ge(s_b2, 16)
            nc.gpsimd.tensor_copy(b2_cut[:, 0, :], b2_rows[:, :]).then_inc(b2_step, 1)
            pool.wait_ge(b2_step, 1)
            nc.gpsimd.tensor_tensor(b2_rest[:, 0, :], b2_rows[:, :], b2_cut[:, 0, :], ALU.subtract).then_inc(b2_step, 1)
            pool.wait_ge(b2_step, 2)
            nc.gpsimd.tensor_copy(b2_cut[:, 1, :], b2_rest[:, 0, :]).then_inc(b2_step, 1)
            pool.wait_ge(b2_step, 3)
            nc.gpsimd.tensor_tensor(b2_rest[:, 1, :], b2_rest[:, 0, :], b2_cut[:, 1, :], ALU.subtract).then_inc(b2_step, 1)
            pool.wait_ge(b2_step, 4)
            nc.gpsimd.tensor_copy(b2_cut[:, 2, :], b2_rest[:, 1, :]).then_inc(b2_step, 1)
            pool.wait_ge(ids_ready, 1)
            pool.wait_ge(s_w1, 16)

            def turn(i, first, last):
                for j in range(UNROLL):
                    t = i * UNROLL + j
                    lang = lang_of(pool, t)
                    if not (first and j < 2):
                        pool.wait_ge(h_summed, t - 1)
                    nc.gpsimd.tensor_copy(w1_now[:, j % 2, :, :],
                                          w1_all[:, bass.ds(lang, 1), :, :].rearrange("p o c a -> p (o c) a"))\
                        .then_inc(w1_staged, 1)
                    if first and j == 0:
                        pool.wait_ge(s_beta, 16)
                    if j % 2 == 0:
                        pool.wait_ge(x_loaded[j // 2], 16 * (i + 1))
                    if not first:
                        pool.wait_ge(out_ready, t - UNROLL + 1)
                    nc.gpsimd.tensor_tensor(x_beta[:, j, :], x_in[:, j, :], of_lang(beta_all, lang), ALU.add)\
                        .then_inc(x_beta_ready, 1)

            all_turns(pool, turn)

        @block.scalar
        def _(act):
            act.dma_start(b2_rows[:, :], b2).then_inc(s_b2, 16)
            act.dma_start(b1_all[:, :], b1.rearrange("l a -> a l"), allow_slow_non_contiguous=True).then_inc(s_b1, 16)
            act.wait_ge(b2_step, 5)
            for k in range(3):
                act.dma_start(b2_parts[k:k + 1, :, :], b2_cut[:, k, :]).then_inc(b2_ready, 16)
            act.wait_ge(ids_ready, 1)

            def copy_x_T(t, j, fresh):
                act.wait_ge(x_turned, t + 1)
                if not fresh:
                    act.wait_ge(h_summed, t - 1)
                nc.scalar.copy(x_T[:, j % 2, :, :], ps_T[j % 2][:, :, :]).then_inc(x_T_ready, 1)

            def relu(t, j, fresh):
                lang = lang_of(act, t)
                act.wait_ge(h_summed, t + 1)
                if not fresh:
                    act.wait_ge(adapted, t - 1)
                nc.scalar.activation(h_T[:, j % 2, :], ps_h[j % 2][:, 0:S], ACT.Relu,
                                     bias=b1_all[:, bass.ds(lang, 1)]).then_inc(h_T_ready, 1)

            def square(t, j):
                act.wait_ge(y_ready, t + 1)
                nc.scalar.activation(squares[:, j % 2, :], ps_y[j % Y_BANKS][:, :], ACT.Square, scale=-float(H),
                                     bias=row_sum[:, j:j + 1], accum_out=sq_sum[:, j:j + 1]).then_inc(squared, 1)

            def root(t, j):
                act.wait_ge(squared, t + 1)
                nc.scalar.activation(std[:, j - 1:j + 1], sq_sum[:, j - 1:j + 1], ACT.Sqrt, scale=float(H) ** -3,
                                     bias=eps[:, 0:1]).then_inc(std_ready, 1)

            def turn(i, first, last):
                for j in range(UNROLL):
                    t = i * UNROLL + j
                    if not (last and j == UNROLL - 1):
                        copy_x_T(t + 1, (j + 1) % UNROLL, first and j < 1)
                    if first and j == 0:
                        act.wait_ge(s_b1, 16)
                    relu(t, j, first and j < 2)
                    if not (first and j < 2):
                        square(t - 2, (j - 2) % UNROLL)
                        if j % 2 == 1:
                            root(t - 2, (j - 2) % UNROLL)

            copy_x_T(0, 0, True)
            all_turns(act, turn)
            square(B - 2, UNROLL - 2)
            square(B - 1, UNROLL - 1)
            root(B - 1, UNROLL - 1)

        @block.tensor
        def _(pe):
            def turn_x(t, i, j):
                if j % 2 == 0:
                    pe.wait_ge(x_loaded[j // 2], 16 * (i + 1))
                for c in range(C):
                    last = nc.tensor.transpose(ps_T[j % 2][:, c, :], x_in[:, j, c * 128:(c + 1) * 128], identity[:, :])
                last.then_inc(x_turned, 1)

            def first_product(t, j):
                pe.wait_ge(w1_staged, t + 1)
                pe.wait_ge(x_T_ready, t + 1)
                for c in range(C):
                    last = nc.tensor.matmul(ps_h[j % 2][:, 0:S], w1_now[:, j % 2, c, :], x_T[:, j % 2, c, :],
                                            start=(c == 0), stop=(c == C - 1))
                last.then_inc(h_summed, 1)

            def second_product(t, j, fresh):
                lang = lang_of(pe, t)
                if not fresh:
                    pe.wait_ge(out_ready, t - Y_BANKS + 1)
                nc.tensor.matmul(ps_y[j % Y_BANKS][:, :], ones[:, :], of_lang(b2_parts, lang), start=True, stop=False)
                pe.wait_ge(h_T_ready, t + 1)
                nc.tensor.matmul(ps_y[j % Y_BANKS][:, :], h_T[:, j % 2, :], of_lang(w2_all, lang),
                                 start=False, stop=True).then_inc(adapted, 1)

            def turn(i, first, last):
                for j in range(UNROLL):
                    t = i * UNROLL + j
                    if not (last and j == UNROLL - 1):
                        turn_x(t + 1, i + (j + 1) // UNROLL, (j + 1) % UNROLL)
                    first_product(t, j)
                    if first and j == 1:
                        pe.wait_ge(b2_ready, 48)
                        pe.wait_ge(s_w2, 16)
                    if not (first and j == 0):
                        second_product(t - 1, (j - 1) % UNROLL, first and j - 1 < Y_BANKS)

            pe.wait_ge(identity_ready, 1)
            pe.wait_ge(ids_ready, 1)
            turn_x(0, 0, 0)
            all_turns(pe, turn)
            second_product(B - 1, UNROLL - 1, False)

        @block.vector
        def _(dve):
            dve.wait_ge(s_ids, 16)
            nc.vector.tensor_scalar(ids_fix[:, 0, :], ids_raw[:, :], 0.0, float(L), ALU.is_lt, ALU.mult).then_inc(ids_step, 1)
            dve.wait_ge(ids_step, 1)
            nc.vector.tensor_tensor(ids_fix[:, 1, :], ids_raw[:, :], ids_fix[:, 0, :], ALU.add).then_inc(ids_step, 1)
            dve.wait_ge(ids_step, 2)
            nc.vector.tensor_scalar(lang_ids[:, :], ids_fix[:, 1, :], 0.0, float(L - 1), ALU.max, ALU.min).then_inc(ids_ready, 1)
            dve.wait_ge(ids_ready, 1)

            def add_x(t, j):
                dve.wait_ge(adapted, t + 1)
                bank = ps_y[j % Y_BANKS][:, :]
                nc.vector.scalar_tensor_tensor(bank, bank, 1.0, x_in[:, j, :], ALU.mult, ALU.add,
                                               accum_out=row_sum[:, j:j + 1]).then_inc(y_ready, 1)

            def means(t, j):
                dve.wait_ge(y_ready, t + 1)
                nc.vector.tensor_scalar(mean[:, j - 1:j + 1], row_sum[:, j - 1:j + 1], 1.0 / H, None, ALU.mult)\
                    .then_inc(mean_ready, 1)

            def invert(q, j):
                dve.wait_ge(std_ready, q + 1)
                nc.vector.reciprocal(rstd[:, j:j + 2], std[:, j:j + 2]).then_inc(rstd_ready, 1)

            def scale(t, q, j):
                lang = lang_of(dve, t)
                if j % 2 == 0:
                    dve.wait_ge(mean_ready, q + 1)
                    dve.wait_ge(squared, t + 2)
                bank = ps_y[j % Y_BANKS][:, :]
                nc.vector.scalar_tensor_tensor(bank, bank, mean[:, j:j + 1], of_lang(gamma_all, lang),
                                               ALU.subtract, ALU.mult).then_inc(scaled, 1)

            def finish(t, i, q, j, fresh):
                if j % 2 == 0:
                    dve.wait_ge(rstd_ready, q + 1)
                    if not fresh:
                        dve.wait_ge(stored[j // 2], 16 * i)
                dve.wait_ge(scaled, t + 1)
                dve.wait_ge(x_beta_ready, t + 1)
                nc.vector.scalar_tensor_tensor(y_out[:, j, :], ps_y[j % Y_BANKS][:, :], rstd[:, j:j + 1],
                                               x_beta[:, j, :], ALU.mult, ALU.add).then_inc(out_ready, 1)

            def step(i, j, first, has_sum, has_norm, fresh):
                t = i * UNROLL + j
                late, late_i = (j - 4) % UNROLL, i + (j - 4) // UNROLL
                q = late_i * PAIRS + late // 2
                if has_norm:
                    if late % 2 == 0:
                        invert(q, late)
                    scale(t - 4, q, late)
                if has_sum:
                    add_x(t - 1, (j - 1) % UNROLL)
                    if (j - 1) % 2 == 1:
                        means(t - 1, (j - 1) % UNROLL)
                if has_norm:
                    finish(t - 4, late_i, q, late, fresh)

            def turn(i, first, last):
                for j in range(UNROLL):
                    if first and j == 4:
                        dve.wait_ge(s_gamma, 16)
                    step(i, j, first, not (first and j == 0), not (first and j < 4), first)

            turn(0, True, False)
            for j in range(UNROLL):
                step(1, j, False, True, True, j < 4)
            with dve.Fori(2, TURNS) as i:
                turn(i, False, False)
            for j in range(4):
                step(TURNS, j, False, j == 0, True, False)


INPUTS = ["x", "itok_B_0_8", "L0_cond_W1", "L0_cond_b1", "L0_cond_W2", "L0_cond_b2", "L0_cond_gamma", "L0_cond_beta"]


def kernel(**inputs):
    import numpy as np
    import concourse.bacc as bacc
    from concourse.bass_utils import run_bass_kernel_spmd

    nc = bacc.Bacc("TRN2", target_bir_lowering=False, num_devices=1)
    arrays, args = {}, []
    for name in INPUTS:
        a = np.ascontiguousarray(inputs[name])
        arrays[f"in_{name}"] = a
        args.append(nc.dram_tensor(f"in_{name}", a.shape, mybir.dt.from_np(a.dtype), kind="ExternalInput").ap())
    out = nc.dram_tensor("out", inputs["x"].shape, F32, kind="ExternalOutput").ap()
    build(nc, *args, out)
    return run_bass_kernel_spmd(nc, [arrays], core_ids=[0]).results[0]["out"]
```

```python
from contextlib import ExitStack

import concourse.bass as bass
from concourse import mybir

F32 = mybir.dt.float32
F32R = mybir.dt.float32r
BF16 = mybir.dt.bfloat16
I32 = mybir.dt.int32
ALU = mybir.AluOpType
ACT = mybir.ActivationFunctionType

LN_EPS = 1e-5
UNROLL = 8
PAIRS = UNROLL // 2
Y_BANKS = 4
LAG = 3
H_SLOTS = 4


def build(nc, x, ids, w1, b1, w2, b2, gamma, beta, out):
    B, S, H = x.shape
    L, _, A = w1.shape
    C = H // 128
    TURNS = B // UNROLL
    W2_CHUNKS = 5
    LC = L // W2_CHUNKS
    assert S == 128 and A == 128 and H == 512 and B % UNROLL == 0 and TURNS > 2

    x_pairs = x.rearrange("(n b) s h -> s n b h", b=2)
    out_pairs = out.rearrange("(n b) s h -> s n b h", b=2)

    with ExitStack() as ctx:
        def sb(name, shape, dt):
            return ctx.enter_context(nc.sbuf_tensor(name, shape, dt))

        def psum(name, shape, dt):
            return ctx.enter_context(nc.psum_tensor(name, shape, dt))

        def sem(name):
            return ctx.enter_context(nc.semaphore(name))

        w1_all = sb("w1_all", [128, L, C, A], F32)
        w2_all = sb("w2_all", [128, L, H], F32)
        w2_high = sb("w2_high", [128, L, H], F32R)
        w2_low = sb("w2_low", [128, L, H], F32R)
        gamma_all = sb("gamma_all", [128, L, H], F32)
        beta_all = sb("beta_all", [128, L, H], F32)
        b1_all = sb("b1_all", [128, L], F32)
        rows = sb("rows", [3 * L, H], F32)
        rest = sb("rest", [3 * L, 2, H], F32)
        cut = sb("cut", [3 * L, 3, H], BF16)
        parts = sb("parts", [128, H], BF16)
        pick_row = sb("pick_row", [128, 3 * L], BF16)
        pick = sb("pick", [128, 3 * L, 128], BF16)
        identity = sb("identity", [128, 128], F32)
        ids_raw = sb("ids_raw", [1, B], I32)
        ids_fix = sb("ids_fix", [1, 2, B], F32)
        lang_ids = sb("lang_ids", [1, B], I32)
        eps = sb("eps", [128, 1], F32)
        x_in = sb("x_in", [128, UNROLL, H], F32)
        x_beta = sb("x_beta", [128, UNROLL, H], F32)
        x_T = sb("x_T", [128, 2, C, S], F32)
        h_rows = sb("h_rows", [128, 2, A], F32)
        h_T = sb("h_T", [128, H_SLOTS, S], F32)
        h_high = sb("h_high", [128, H_SLOTS, S], F32R)
        h_low = sb("h_low", [128, H_SLOTS, S], F32R)
        y_out = sb("y_out", [128, UNROLL, H], F32)
        squares = sb("squares", [128, 2, H], F32)
        row_sum = sb("row_sum", [128, UNROLL], F32)
        mean = sb("mean", [128, UNROLL], F32)
        sq_sum = sb("sq_sum", [128, UNROLL], F32)
        std = sb("std", [128, UNROLL], F32)
        rstd = sb("rstd", [128, UNROLL], F32)

        ps_T = [psum(f"ps_T{i}", [128, C, S], F32) for i in range(2)]
        ps_h = psum("ps_h", [128, H], F32)
        ps_hT = psum("ps_hT", [128, H], F32)
        ps_y = [psum(f"ps_y{i}", [128, H], F32) for i in range(Y_BANKS)]

        s_ids = sem("s_ids")
        s_b1 = sem("s_b1")
        s_rows = sem("s_rows")
        s_w1 = [sem(f"s_w1_{half}") for half in range(2)]
        s_w2 = [sem(f"s_w2_{n}") for n in range(W2_CHUNKS)]
        w2_high_ready = sem("w2_high_ready")
        w2_low_ready = sem("w2_low_ready")
        x_loaded = [sem(f"x_loaded{i}") for i in range(PAIRS)]
        ids_step = sem("ids_step")
        ids_ready = sem("ids_ready")
        set_ready = sem("set_ready")
        parts_zero = sem("parts_zero")
        identity_ready = sem("identity_ready")
        pick_step = sem("pick_step")
        pick_ready = sem("pick_ready")
        cut_step = sem("cut_step")
        parts_ready = sem("parts_ready")
        spread = sem("spread")
        spread_act = sem("spread_act")
        spread_dve = sem("spread_dve")
        x_beta_ready = sem("x_beta_ready")
        x_turned = sem("x_turned")
        x_T_ready = sem("x_T_ready")
        h_summed = sem("h_summed")
        h_rows_ready = sem("h_rows_ready")
        h_turned = sem("h_turned")
        h_high_ready = sem("h_high_ready")
        h_T_ready = sem("h_T_ready")
        h_low_ready = sem("h_low_ready")
        adapted = sem("adapted")
        y_ready = sem("y_ready")
        squared = sem("squared")
        scaled = sem("scaled")
        out_ready = sem("out_ready")
        mean_ready = sem("mean_ready")
        std_ready = sem("std_ready")
        rstd_ready = sem("rstd_ready")
        stored = [sem(f"stored{i}") for i in range(PAIRS)]

        block = ctx.enter_context(nc.Block())

        def langs_of(engine, t, n):
            return nc.values_load_multi_w_load_instructions(
                lang_ids[0:1, bass.ds(t, n)], engines=[engine.engine], min_val=0, max_val=L - 1,
                skip_runtime_bounds_check_because="VectorE keeps lang_ids within the tables")[1]

        def spread_to(n):
            return (gamma_all if n < L else beta_all)[:, n % L, :]

        def of_lang(table, lang):
            return table[:, bass.ds(lang, 1), :].rearrange("p o h -> p (o h)")

        def all_turns(engine, turn):
            turn(0, True, False)
            with engine.Fori(1, TURNS - 1) as i:
                turn(i, False, False)
            turn(TURNS - 1, False, True)

        @block.sync
        def _(sp):
            sp.dma_start(ids_raw[:, :], ids.rearrange("(a b) -> a b", a=1)).then_inc(s_ids, 16)
            for k, table in enumerate((b2, gamma, beta)):
                sp.dma_start(rows[k * L:(k + 1) * L, :], table).then_inc(s_rows, 16)
            sp.dma_start(x_in[:, 0:2, :], x_pairs[:, 0, :, :]).then_inc(x_loaded[0], 16)
            def load_w1(half):
                langs = slice(half * L // 2, (half + 1) * L // 2)
                sp.dma_start(w1_all[:, langs, :, :], w1[langs].rearrange("l (c p) a -> p l c a", p=128))\
                    .then_inc(s_w1[half], 16)

            load_w1(0)
            sp.wait_ge(parts_zero, 1)
            for k in range(3):
                sp.wait_ge(cut_step, 2 * k + 1)
                sp.dma_start(parts[32 * k:32 * k + 3 * L, :], cut[:, k, :]).then_inc(parts_ready, 16)
            load_w1(1)
            sp.dma_start(x_in[:, 2:4, :], x_pairs[:, 1, :, :]).then_inc(x_loaded[1], 16)
            for n in range(W2_CHUNKS):
                sp.dma_start(w2_all[:, n * LC:(n + 1) * LC, :], w2[n * LC:(n + 1) * LC].rearrange("l a h -> a l h"))\
                    .then_inc(s_w2[n], 16)
            for k in range(2, PAIRS):
                sp.dma_start(x_in[:, 2 * k:2 * k + 2, :], x_pairs[:, k, :, :]).then_inc(x_loaded[k], 16)

            def load_pair(i, k):
                sp.wait_ge(y_ready, (i - 1) * UNROLL + 2 * k + 2)
                sp.wait_ge(x_beta_ready, (i - 1) * UNROLL + 2 * k + 2)
                sp.dma_start(x_in[:, 2 * k:2 * k + 2, :],
                             x_pairs[:, bass.ds(i * PAIRS + k, 1), :, :].rearrange("s o b h -> s (o b) h"))\
                    .then_inc(x_loaded[k], 16)

            def store_pair(i, k):
                sp.wait_ge(out_ready, i * UNROLL + 2 * k + 2)
                sp.dma_start(out_pairs[:, bass.ds(i * PAIRS + k, 1), :, :].rearrange("s o b h -> s (o b) h"),
                             y_out[:, 2 * k:2 * k + 2, :]).then_inc(stored[k], 16)

            def turn(i, first, last):
                for k in range(PAIRS):
                    if not last:
                        load_pair(i + 1, k)
                    if not (first and k < 2):
                        store_pair(i - 1 if k < 2 else i, (k - 2) % PAIRS)

            all_turns(sp, turn)
            for k in range(PAIRS - 2, PAIRS):
                store_pair(TURNS - 1, k)
            for k in range(PAIRS):
                sp.wait_ge(stored[k], 16 * TURNS)

        @block.gpsimd
        def _(pool):
            nc.gpsimd.memset(parts[:, :], 0.0).then_inc(parts_zero, 1)
            nc.gpsimd.memset(identity[:, :], 0.0).then_inc(set_ready, 1)
            nc.gpsimd.memset(pick_row[:, :], 0.0).then_inc(set_ready, 1)
            nc.gpsimd.memset(eps[:, :], LN_EPS).then_inc(set_ready, 1)
            pool.wait_ge(set_ready, 3)
            for g in range(3):
                nc.gpsimd.affine_select(out=pick_row[:, :], in_=pick_row[:, :], compare_op=ALU.not_equal, fill=1.0,
                                        base=-32 * g, pattern=[[-1, 3 * L]], channel_multiplier=1).then_inc(pick_step, 1)
                pool.wait_ge(pick_step, g + 1)
            nc.gpsimd.affine_select(out=identity[:, :], in_=identity[:, :], compare_op=ALU.not_equal, fill=1.0,
                                    base=0, pattern=[[-1, 128]], channel_multiplier=1).then_inc(identity_ready, 1)
            def low_h(t, j):
                pool.wait_ge(h_high_ready, t + 1)
                pool.wait_ge(h_T_ready, t + 1)
                nc.gpsimd.tensor_tensor(h_low[:, j % H_SLOTS, :], h_T[:, j % H_SLOTS, :], h_high[:, j % H_SLOTS, :].bitcast(F32),
                                        ALU.subtract).then_inc(h_low_ready, 1)

            pool.wait_ge(ids_ready, 1)
            pool.wait_ge(spread_act, L)
            pool.wait_ge(spread_dve, L)

            def turn(i, first, last):
                langs = langs_of(pool, i * UNROLL, UNROLL)
                for j in range(UNROLL):
                    t = i * UNROLL + j
                    lang = langs[j]
                    if j % 2 == 0:
                        pool.wait_ge(x_loaded[j // 2], 16 * (i + 1))
                    if not first:
                        pool.wait_ge(out_ready, t - UNROLL + 1)
                    nc.gpsimd.tensor_tensor(x_beta[:, j, :], x_in[:, j, :], of_lang(beta_all, lang), ALU.add)\
                        .then_inc(x_beta_ready, 1)
                    if not (first and j == 0):
                        low_h(t - 1, (j - 1) % UNROLL)

            all_turns(pool, turn)
            low_h(B - 1, UNROLL - 1)

        @block.scalar
        def _(act):
            act.dma_start(b1_all[:, :], b1.rearrange("l a -> a l"), allow_slow_non_contiguous=True).then_inc(s_b1, 16)
            act.wait_ge(pick_step, 3)
            for k in (1, 2, 0):
                nc.scalar.copy(pick[:, k * L:(k + 1) * L, :],
                               pick_row[:, k * L:(k + 1) * L].unsqueeze(2).broadcast_to([128, L, 128])).then_inc(pick_ready, 1)
            for n in range(0, 2 * L, 2):
                act.wait_ge(spread, n + 1)
                nc.scalar.copy(spread_to(n), ps_y[n % Y_BANKS][:, :]).then_inc(spread_act, 1)
            act.wait_ge(ids_ready, 1)

            def copy_x_T(t, j, fresh):
                act.wait_ge(x_turned, t + 1)
                if not fresh:
                    act.wait_ge(h_summed, t - 1)
                nc.scalar.copy(x_T[:, j % 2, :, :], ps_T[j % 2][:, :, :]).then_inc(x_T_ready, 1)

            def copy_h(t, j):
                act.wait_ge(h_summed, t + 1)
                nc.scalar.copy(h_rows[:, j % 2, :], ps_h[:, 0:A]).then_inc(h_rows_ready, 1)

            def relu(t, j, lang, fresh):
                act.wait_ge(h_turned, t + 1)
                if not fresh:
                    act.wait_ge(adapted, t - H_SLOTS + 1)
                bias = b1_all[:, bass.ds(lang, 1)]
                nc.scalar.activation(h_high[:, j % H_SLOTS, :], ps_hT[:, 0:S], ACT.Relu, bias=bias).then_inc(h_high_ready, 1)
                nc.scalar.activation(h_T[:, j % H_SLOTS, :], ps_hT[:, 0:S], ACT.Relu, bias=bias).then_inc(h_T_ready, 1)

            def square(t, j):
                act.wait_ge(y_ready, t + 1)
                nc.scalar.activation(squares[:, j % 2, :], ps_y[j % Y_BANKS][:, :], ACT.Square, scale=-float(H),
                                     bias=row_sum[:, j:j + 1], accum_out=sq_sum[:, j:j + 1]).then_inc(squared, 1)

            def root(t, j):
                act.wait_ge(squared, t + 1)
                nc.scalar.activation(std[:, j - 1:j + 1], sq_sum[:, j - 1:j + 1], ACT.Sqrt, scale=float(H) ** -3,
                                     bias=eps[:, 0:1]).then_inc(std_ready, 1)

            def turn(i, first, last):
                behind = 0 if first else 1
                langs = langs_of(act, i * UNROLL - behind, UNROLL - 1 + behind)
                for j in range(UNROLL):
                    t = i * UNROLL + j
                    if not (first and j == 0):
                        relu(t - 1, (j - 1) % UNROLL, langs[j - 1 + behind], first and j - 1 < H_SLOTS)
                    if not (last and j == UNROLL - 1):
                        copy_x_T(t + 1, (j + 1) % UNROLL, first and j < 1)
                    copy_h(t, j)
                    if not (first and j < LAG + 1):
                        norm_sums(t - LAG - 1, (j - LAG - 1) % UNROLL)

            def norm_sums(t, j):
                square(t, j)
                if j % 2 == 1:
                    root(t, j)

            act.wait_ge(s_b1, 16)
            copy_x_T(0, 0, True)
            for n in range(W2_CHUNKS):
                act.wait_ge(s_w2[n], 16)
                nc.scalar.copy(w2_high[:, n * LC:(n + 1) * LC, :], w2_all[:, n * LC:(n + 1) * LC, :])\
                    .then_inc(w2_high_ready, 1)
            all_turns(act, turn)
            relu(B - 1, UNROLL - 1, langs_of(act, B - 1, 1)[0], False)
            for k in range(LAG + 1, 0, -1):
                norm_sums(B - k, UNROLL - k)

        @block.tensor
        def _(pe):
            def turn_x(t, i, j):
                if j % 2 == 0:
                    pe.wait_ge(x_loaded[j // 2], 16 * (i + 1))
                for c in range(C):
                    last = nc.tensor.transpose(ps_T[j % 2][:, c, :], x_in[:, j, c * 128:(c + 1) * 128], identity[:, :])
                last.then_inc(x_turned, 1)

            def first_product(t, j, lang):
                pe.wait_ge(x_T_ready, t + 1)
                for c in range(C):
                    last = nc.tensor.matmul(ps_h[:, 0:A], x_T[:, j % 2, c, :],
                                            w1_all[:, bass.ds(lang, 1), c, :].rearrange("p o a -> p (o a)"),
                                            start=(c == 0), stop=(c == C - 1))
                last.then_inc(h_summed, 1)

            def turn_h(t, j):
                pe.wait_ge(h_rows_ready, t + 1)
                nc.tensor.transpose(ps_hT[:, 0:S], h_rows[:, j % 2, :], identity[:, :]).then_inc(h_turned, 1)

            def second_product(t, j, lang, fresh):
                h = j % H_SLOTS
                if not fresh:
                    pe.wait_ge(out_ready, t - Y_BANKS + 1)
                bank = ps_y[j % Y_BANKS][:, :]
                nc.tensor.matmul(bank, of_lang(pick, lang), parts[:, :], start=True, stop=False)
                pe.wait_ge(h_high_ready, t + 1)
                nc.tensor.matmul(bank, h_high[:, h, :], of_lang(w2_high, lang), start=False, stop=False)
                nc.tensor.matmul(bank, h_high[:, h, :], of_lang(w2_low, lang), start=False, stop=False)
                pe.wait_ge(h_low_ready, t + 1)
                nc.tensor.matmul(bank, h_low[:, h, :], of_lang(w2_high, lang), start=False, stop=True)\
                    .then_inc(adapted, 1)

            def turn(i, first, last):
                behind = 0 if first else LAG
                langs = langs_of(pe, i * UNROLL - behind, UNROLL + behind)
                for j in range(UNROLL):
                    t = i * UNROLL + j
                    if not (first and j == 0):
                        turn_h(t - 1, (j - 1) % UNROLL)
                    if not (last and j == UNROLL - 1):
                        turn_x(t + 1, i + (j + 1) // UNROLL, (j + 1) % UNROLL)
                    first_product(t, j, langs[j + behind])
                    if first and j == LAG:
                        pe.wait_ge(w2_high_ready, W2_CHUNKS)
                        pe.wait_ge(w2_low_ready, W2_CHUNKS)
                    if not (first and j < LAG):
                        second_product(t - LAG, (j - LAG) % UNROLL, langs[j - LAG + behind], first and j - LAG < Y_BANKS)

            pe.wait_ge(identity_ready, 1)
            turn_x(0, 0, 0)
            pe.wait_ge(parts_ready, 48)
            pe.wait_ge(pick_ready, 1)
            for n in range(2 * L):
                if n == L:
                    pe.wait_ge(pick_ready, 2)
                if n >= Y_BANKS:
                    pe.wait_ge(spread_dve if n % 2 else spread_act, (n - Y_BANKS) // 2 + 1)
                nc.tensor.matmul(ps_y[n % Y_BANKS][:, :], pick[:, L + n, :], parts[:, :], start=True, stop=True)\
                    .then_inc(spread, 1)
            pe.wait_ge(ids_ready, 1)
            for half in range(2):
                pe.wait_ge(s_w1[half], 16)
            pe.wait_ge(spread_act, L)
            pe.wait_ge(spread_dve, L)
            pe.wait_ge(pick_ready, 3)
            all_turns(pe, turn)
            turn_h(B - 1, UNROLL - 1)
            langs = langs_of(pe, B - LAG, LAG)
            for k in range(LAG, 0, -1):
                second_product(B - k, UNROLL - k, langs[LAG - k], False)

        @block.vector
        def _(dve):
            dve.wait_ge(s_ids, 16)
            nc.vector.tensor_scalar(ids_fix[:, 0, :], ids_raw[:, :], 0.0, float(L), ALU.is_lt, ALU.mult).then_inc(ids_step, 1)
            dve.wait_ge(ids_step, 1)
            nc.vector.tensor_tensor(ids_fix[:, 1, :], ids_raw[:, :], ids_fix[:, 0, :], ALU.add).then_inc(ids_step, 1)
            dve.wait_ge(ids_step, 2)
            nc.vector.tensor_scalar(lang_ids[:, :], ids_fix[:, 1, :], 0.0, float(L - 1), ALU.max, ALU.min).then_inc(ids_ready, 1)
            dve.wait_ge(s_rows, 3 * 16)
            nc.vector.tensor_copy(cut[:, 0, :], rows[:, :]).then_inc(cut_step, 1)
            dve.wait_ge(cut_step, 1)
            nc.vector.tensor_tensor(rest[:, 0, :], rows[:, :], cut[:, 0, :], ALU.subtract).then_inc(cut_step, 1)
            dve.wait_ge(cut_step, 2)
            nc.vector.tensor_copy(cut[:, 1, :], rest[:, 0, :]).then_inc(cut_step, 1)
            dve.wait_ge(cut_step, 3)
            nc.vector.tensor_tensor(rest[:, 1, :], rest[:, 0, :], cut[:, 1, :], ALU.subtract).then_inc(cut_step, 1)
            dve.wait_ge(cut_step, 4)
            nc.vector.tensor_copy(cut[:, 2, :], rest[:, 1, :]).then_inc(cut_step, 1)
            for n in range(1, 2 * L, 2):
                dve.wait_ge(spread, n + 1)
                nc.vector.tensor_copy(spread_to(n), ps_y[n % Y_BANKS][:, :]).then_inc(spread_dve, 1)
            dve.wait_ge(spread_act, L)
            dve.wait_ge(spread_dve, L)
            for n in range(W2_CHUNKS):
                dve.wait_ge(w2_high_ready, n + 1)
                nc.vector.tensor_tensor(w2_low[:, n * LC:(n + 1) * LC, :], w2_all[:, n * LC:(n + 1) * LC, :],
                                        w2_high[:, n * LC:(n + 1) * LC, :].bitcast(F32), ALU.subtract)\
                    .then_inc(w2_low_ready, 1)
            dve.wait_ge(ids_ready, 1)

            def add_x(t, j):
                dve.wait_ge(adapted, t + 1)
                bank = ps_y[j % Y_BANKS][:, :]
                nc.vector.scalar_tensor_tensor(bank, bank, 1.0, x_in[:, j, :], ALU.mult, ALU.add,
                                               accum_out=row_sum[:, j:j + 1]).then_inc(y_ready, 1)

            def means(t, j):
                dve.wait_ge(y_ready, t + 1)
                nc.vector.tensor_scalar(mean[:, j - 1:j + 1], row_sum[:, j - 1:j + 1], 1.0 / H, None, ALU.mult)\
                    .then_inc(mean_ready, 1)

            def invert(q, j):
                dve.wait_ge(std_ready, q + 1)
                nc.vector.reciprocal(rstd[:, j:j + 2], std[:, j:j + 2]).then_inc(rstd_ready, 1)

            def scale(t, q, j, lang):
                if j % 2 == 0:
                    dve.wait_ge(mean_ready, q + 1)
                    dve.wait_ge(squared, t + 2)
                bank = ps_y[j % Y_BANKS][:, :]
                nc.vector.scalar_tensor_tensor(bank, bank, mean[:, j:j + 1], of_lang(gamma_all, lang),
                                               ALU.subtract, ALU.mult).then_inc(scaled, 1)

            def finish(t, i, q, j, fresh):
                if j % 2 == 0:
                    dve.wait_ge(rstd_ready, q + 1)
                    if not fresh:
                        dve.wait_ge(stored[j // 2], 16 * i)
                dve.wait_ge(scaled, t + 1)
                dve.wait_ge(x_beta_ready, t + 1)
                nc.vector.scalar_tensor_tensor(y_out[:, j, :], ps_y[j % Y_BANKS][:, :], rstd[:, j:j + 1],
                                               x_beta[:, j, :], ALU.mult, ALU.add).then_inc(out_ready, 1)

            def step(i, j, langs, first, has_sum, has_norm, fresh, tail=False):
                t = i * UNROLL + j
                late, late_i = (j - 4) % UNROLL, i + (j - 4) // UNROLL
                q = late_i * PAIRS + late // 2
                if has_norm:
                    if late % 2 == 0:
                        invert(q, late)
                    scale(t - 4, q, late, langs[j] if len(langs) == UNROLL else langs[j % 4])
                if j % 2 == 1 and not (first and j == 1) and not (tail and j == 3):
                    means(t - 2, (j - 2) % UNROLL)
                if has_norm:
                    finish(t - 4, late_i, q, late, fresh)
                if has_sum:
                    add_x(t - 1, (j - 1) % UNROLL)

            langs = langs_of(dve, 0, 4)
            for j in range(UNROLL):
                step(0, j, langs, True, j > 0, j >= 4, True)
            langs = langs_of(dve, UNROLL - 4, UNROLL)
            for j in range(UNROLL):
                step(1, j, langs, False, True, True, j < 4)
            with dve.Fori(2, TURNS) as i:
                langs = langs_of(dve, i * UNROLL - 4, UNROLL)
                for j in range(UNROLL):
                    step(i, j, langs, False, True, True, False)
            langs = langs_of(dve, B - 4, 4)
            for j in range(4):
                step(TURNS, j, langs, False, j == 0, True, False, tail=True)


INPUTS = ["x", "itok_B_0_8", "L0_cond_W1", "L0_cond_b1", "L0_cond_W2", "L0_cond_b2", "L0_cond_gamma", "L0_cond_beta"]


def kernel(**inputs):
    import numpy as np
    import concourse.bacc as bacc
    from concourse.bass_utils import run_bass_kernel_spmd

    nc = bacc.Bacc("TRN2", target_bir_lowering=False, num_devices=1)
    arrays, args = {}, []
    for name in INPUTS:
        a = np.ascontiguousarray(inputs[name])
        arrays[f"in_{name}"] = a
        args.append(nc.dram_tensor(f"in_{name}", a.shape, mybir.dt.from_np(a.dtype), kind="ExternalInput").ap())
    out = nc.dram_tensor("out", inputs["x"].shape, F32, kind="ExternalOutput").ap()
    build(nc, *args, out)
    return run_bass_kernel_spmd(nc, [arrays], core_ids=[0]).results[0]["out"]
```

```python
from contextlib import ExitStack

import concourse.bass as bass
from concourse import mybir

F32 = mybir.dt.float32
F32R = mybir.dt.float32r
BF16 = mybir.dt.bfloat16
I32 = mybir.dt.int32
ALU = mybir.AluOpType
ACT = mybir.ActivationFunctionType

LN_EPS = 1e-5
UNROLL = 16
PAIRS = UNROLL // 2
Y_BANKS = 4
LAG = 4
H_SLOTS = 8
H_T_SLOTS = 4
B2_BY_POOL = (1, 5, 9, 13)
B2_LATE = 2
NORM_LAG = 4


def build(nc, x, ids, w1, b1, w2, b2, gamma, beta, out):
    B, S, H = x.shape
    L, _, A = w1.shape
    C = H // 128
    TURNS = B // UNROLL
    W_CHUNKS = 5
    LC = L // W_CHUNKS
    X_AFTER_W2 = (1, 4)
    assert S == 128 and A == 128 and H == 512 and B % UNROLL == 0 and TURNS > 2

    x_pairs = x.rearrange("(n b) s h -> s n b h", b=2)
    out_pairs = out.rearrange("(n b) s h -> s n b h", b=2)

    with ExitStack() as ctx:
        def sb(name, shape, dt):
            return ctx.enter_context(nc.sbuf_tensor(name, shape, dt))

        def psum(name, shape, dt):
            return ctx.enter_context(nc.psum_tensor(name, shape, dt))

        def sem(name):
            return ctx.enter_context(nc.semaphore(name))

        w1_all = sb("w1_all", [128, L, C, A], F32)
        w2_all = sb("w2_all", [128, L, H], F32)
        w2_high = sb("w2_high", [128, L, H], F32R)
        w2_low = sb("w2_low", [128, L, H], F32R)
        gamma_all = sb("gamma_all", [128, L, H], F32)
        b2_all = sb("b2_all", [128, L, H], F32)
        x_b2 = sb("x_b2", [128, 2, H], F32)
        beta_all = sb("beta_all", [128, L, H], F32)
        b1_all = sb("b1_all", [128, L], F32)
        rows = sb("rows", [3 * L, H], F32)
        cut = sb("cut", [128, 3, H], BF16)
        parts = sb("parts", [128, H], BF16)
        pick_row = sb("pick_row", [128, 3 * L], BF16)
        pick = sb("pick", [128, 3 * L, 128], BF16)
        identity = sb("identity", [128, 128], F32)
        ids_raw = sb("ids_raw", [1, B], I32)
        ids_fix = sb("ids_fix", [1, 2, B], F32)
        lang_ids = sb("lang_ids", [1, B], I32)
        eps = sb("eps", [128, 1], F32)
        x_io = sb("x_io", [128, UNROLL, H], F32)
        x_T = sb("x_T", [128, 2, C, S], F32)
        h_rows = sb("h_rows", [128, 2, A], F32)
        h_T = sb("h_T", [128, H_T_SLOTS, S], F32)
        h_high = sb("h_high", [128, H_SLOTS, S], F32R)
        h_low = sb("h_low", [128, H_SLOTS, S], F32R)
        squares = cut
        row_sum = sb("row_sum", [128, UNROLL], F32)
        mean = sb("mean", [128, UNROLL], F32)
        sq_sum = sb("sq_sum", [128, UNROLL], F32)
        table_load = sb("table_load", [128, 1], F32)
        std = sb("std", [128, UNROLL], F32)
        rstd = sb("rstd", [128, UNROLL], F32)

        ps_T = [psum(f"ps_T{i}", [128, C, S], F32) for i in range(2)]
        ps_h = psum("ps_h", [128, H], F32)
        ps_hT = psum("ps_hT", [128, H], F32)
        ps_y = [psum(f"ps_y{i}", [128, H], F32) for i in range(Y_BANKS)]

        s_ids = sem("s_ids")
        s_b1 = sem("s_b1")
        s_rows = sem("s_rows")
        s_b2 = sem("s_b2")
        x_b2_ready = sem("x_b2_ready")
        s_w1 = sem("s_w1")
        s_w2 = [sem(f"s_w2_{n}") for n in range(W_CHUNKS)]
        w2_high_ready = sem("w2_high_ready")
        w2_low_ready = sem("w2_low_ready")
        x_loaded = [sem(f"x_loaded{i}") for i in range(PAIRS)]
        ids_step = sem("ids_step")
        ids_ready = sem("ids_ready")
        set_ready = sem("set_ready")
        parts_zero = sem("parts_zero")
        identity_ready = sem("identity_ready")
        pick_step = sem("pick_step")
        pick_ready = sem("pick_ready")
        cut_step = sem("cut_step")
        parts_ready = sem("parts_ready")
        spread = sem("spread")
        spread_act = sem("spread_act")
        spread_dve = sem("spread_dve")
        x_beta_ready = sem("x_beta_ready")
        x_turned = sem("x_turned")
        x_T_ready = sem("x_T_ready")
        h_summed = sem("h_summed")
        h_rows_ready = sem("h_rows_ready")
        h_turned = sem("h_turned")
        h_high_ready = sem("h_high_ready")
        h_T_ready = sem("h_T_ready")
        h_low_ready = sem("h_low_ready")
        adapted = sem("adapted")
        y_ready = sem("y_ready")
        squared = sem("squared")
        scaled = sem("scaled")
        out_ready = sem("out_ready")
        mean_ready = sem("mean_ready")
        std_ready = sem("std_ready")
        rstd_ready = sem("rstd_ready")
        stored = [sem(f"stored{i}") for i in range(PAIRS)]

        block = ctx.enter_context(nc.Block())

        def langs_of(engine, t, n):
            return nc.values_load_multi_w_load_instructions(
                lang_ids[0:1, bass.ds(t, n)], engines=[engine.engine], min_val=0, max_val=L - 1,
                skip_runtime_bounds_check_because="VectorE keeps lang_ids within the tables")[1]

        def seconds_done(j, first, last):
            if j < 0:
                return 0 if first else j - LAG + 1
            if first:
                return max(0, j - LAG + 1)
            if last:
                return min(j, j - LAG + 1 + (j + 1) // (UNROLL // (LAG - 1)))
            return j - LAG + 1

        def seconds(j, first, last):
            return range(seconds_done(j - 1, first, last), seconds_done(j, first, last))

        LEFT = B - seconds_done(UNROLL - 1, False, True) - (TURNS - 1) * UNROLL
        LEFT_NORMS = B - seconds_done(UNROLL - 2, False, True) - (TURNS - 1) * UNROLL

        def spread_to(n):
            return (gamma_all if n < L else beta_all)[:, n % L, :]

        def b2_by_pool(j, first):
            return j in B2_BY_POOL[B2_LATE if first else 0:]

        def b2_slot(j):
            return B2_BY_POOL.index(j) % 2

        def b2_count(i, j):
            return i * len(B2_BY_POOL) + B2_BY_POOL.index(j) + 1 - B2_LATE

        def w2_chunk(table, n):
            return table[:, n * LC:(n + 1) * LC, :]

        def of_lang(table, lang):
            return table[:, bass.ds(lang, 1), :].rearrange("p o h -> p (o h)")

        def all_turns(engine, turn):
            turn(0, True, False)
            with engine.Fori(1, TURNS - 1) as i:
                turn(i, False, False)
            turn(TURNS - 1, False, True)

        @block.sync
        def _(sp):
            sp.dma_start(ids_raw[:, :], ids.rearrange("(a b) -> a b", a=1)).then_inc(s_ids, 16)
            for k, table in enumerate((b2, gamma, beta)):
                sp.dma_start(rows[k * L:(k + 1) * L, :], table).then_inc(s_rows, 16)

            def first_x(k):
                sp.dma_start(x_io[:, 2 * k:2 * k + 2, :], x_pairs[:, k, :, :]).then_inc(x_loaded[k], 16)

            first_x(0)
            for n in range(W_CHUNKS):
                langs = slice(n * LC, (n + 1) * LC)
                sp.dma_start(w1_all[:, langs, :, :], w1[langs].rearrange("l (c p) a -> p l c a", p=128)).then_inc(s_w1, 16)
                if n == 1:
                    sp.wait_ge(parts_zero, 1)
                    for k in range(3):
                        sp.wait_ge(cut_step, 2 * k + 1)
                        sp.dma_start(parts[32 * k:32 * k + 3 * L, :], cut[0:3 * L, k, :]).then_inc(parts_ready, 16)
            first_x(1)
            for n in range(W_CHUNKS):
                sp.dma_start(w2_chunk(w2_all, n), w2[n * LC:(n + 1) * LC].rearrange("l a h -> a l h"))\
                    .then_inc(s_w2[n], 16)
                if n in X_AFTER_W2:
                    first_x(2 + X_AFTER_W2.index(n))
            for k in range(2 + len(X_AFTER_W2), PAIRS):
                first_x(k)
            sp.dma_start(b2_all[:, :, :], b2.partition_broadcast(128)).then_inc(s_b2, 16)

            def store_pair(i, k):
                sp.wait_ge(out_ready, i * UNROLL + 2 * k + 2)
                sp.dma_start(out_pairs[:, bass.ds(i * PAIRS + k, 1), :, :].rearrange("s o b h -> s (o b) h"),
                             x_io[:, 2 * k:2 * k + 2, :]).then_inc(stored[k], 16)

            def load_pair(i, k):
                sp.wait_ge(stored[k], 16 * i)
                sp.dma_start(x_io[:, 2 * k:2 * k + 2, :],
                             x_pairs[:, bass.ds(i * PAIRS + k, 1), :, :].rearrange("s o b h -> s (o b) h"))\
                    .then_inc(x_loaded[k], 16)

            def turn(i, first, last):
                for k in range(PAIRS):
                    if last and k == PAIRS - 1:
                        for b in range(2):
                            sp.wait_ge(out_ready, B - 1 + b)
                            sp.dma_start(out[B - 2 + b], x_io[:, UNROLL - 2 + b, :]).then_inc(stored[k], 16)
                        continue
                    store_pair(i, k)
                    if k == 0 and not first:
                        load_pair(i, PAIRS - 1)
                    elif k > 0 and not last:
                        load_pair(i + 1, k - 1)

            all_turns(sp, turn)
            for k in range(PAIRS):
                sp.wait_ge(stored[k], 16 * (TURNS + (k == PAIRS - 1)))

        @block.gpsimd
        def _(pool):
            nc.gpsimd.memset(parts[:, :], 0.0).then_inc(parts_zero, 1)
            nc.gpsimd.memset(identity[:, :], 0.0).then_inc(set_ready, 1)
            nc.gpsimd.memset(pick_row[:, :], 0.0).then_inc(set_ready, 1)
            nc.gpsimd.memset(eps[:, :], LN_EPS).then_inc(set_ready, 1)
            pool.wait_ge(set_ready, 3)
            for g in range(3):
                nc.gpsimd.affine_select(out=pick_row[:, :], in_=pick_row[:, :], compare_op=ALU.not_equal, fill=1.0,
                                        base=-32 * g, pattern=[[-1, 3 * L]], channel_multiplier=1).then_inc(pick_step, 1)
                pool.wait_ge(pick_step, g + 1)
            nc.gpsimd.affine_select(out=identity[:, :], in_=identity[:, :], compare_op=ALU.not_equal, fill=1.0,
                                    base=0, pattern=[[-1, 128]], channel_multiplier=1).then_inc(identity_ready, 1)

            def low_h(t, j):
                pool.wait_ge(h_high_ready, t + 1)
                pool.wait_ge(h_T_ready, t + 1)
                nc.gpsimd.tensor_tensor(h_low[:, j % H_SLOTS, :], h_T[:, j % H_T_SLOTS, :],
                                        h_high[:, j % H_SLOTS, :].bitcast(F32), ALU.subtract).then_inc(h_low_ready, 1)

            pool.wait_ge(ids_ready, 1)
            pool.wait_ge(spread_act, L)
            pool.wait_ge(spread_dve, L)

            def add_beta(t, j, lang):
                pool.wait_ge(y_ready, t + 1)
                nc.gpsimd.tensor_tensor(x_io[:, j, :], x_io[:, j, :], of_lang(beta_all, lang), ALU.add)\
                    .then_inc(x_beta_ready, 1)

            def add_b2(t, j, lang, fresh):
                if not fresh:
                    pool.wait_ge(y_ready, t - 7)
                nc.gpsimd.tensor_tensor(x_b2[:, b2_slot(j), :], x_io[:, j, :], of_lang(b2_all, lang), ALU.add)\
                    .then_inc(x_b2_ready, 1)

            def turn(i, first, last):
                behind = 0 if first else LAG + 1
                langs = langs_of(pool, i * UNROLL - behind, UNROLL - 1 + behind)
                for j in range(UNROLL):
                    t = i * UNROLL + j
                    if not (first and j == 0):
                        low_h(t - 1, (j - 1) % UNROLL)
                    if b2_by_pool(j - 1, first):
                        if first:
                            pool.wait_ge(s_b2, 16)
                        add_b2(t - 1, j - 1, langs[j - 1 + behind], first)
                    for u in seconds(j - 1, first, last):
                        add_beta(i * UNROLL + u, u % UNROLL, langs[u + behind])

            all_turns(pool, turn)
            low_h(B - 1, UNROLL - 1)
            langs = langs_of(pool, B - LEFT_NORMS, LEFT_NORMS)
            for k in range(LEFT_NORMS, 0, -1):
                add_beta(B - k, UNROLL - k, langs[LEFT_NORMS - k])

        @block.scalar
        def _(act):
            act.dma_start(b1_all[:, :], b1.rearrange("l a -> a l"), allow_slow_non_contiguous=True).then_inc(s_b1, 16)
            act.wait_ge(set_ready, 3)
            nc.scalar.activation(table_load[:, :], eps[:, :], ACT.Sqrt, bias=eps[:, 0:1])
            act.wait_ge(pick_step, 3)
            for k in (1, 2, 0):
                nc.scalar.copy(pick[:, k * L:(k + 1) * L, :],
                               pick_row[:, k * L:(k + 1) * L].unsqueeze(2).broadcast_to([128, L, 128])).then_inc(pick_ready, 1)
            act.wait_ge(ids_ready, 1)
            first_langs = langs_of(act, 0, UNROLL - 1)
            for n in range(0, 2 * L, 2):
                act.wait_ge(spread, n + 1)
                nc.scalar.copy(spread_to(n), ps_y[n % Y_BANKS][:, :]).then_inc(spread_act, 1)

            def copy_x_T(t, j, fresh):
                act.wait_ge(x_turned, t + 1)
                if not fresh:
                    act.wait_ge(h_summed, t - 1)
                nc.scalar.copy(x_T[:, j % 2, :, :], ps_T[j % 2][:, :, :]).then_inc(x_T_ready, 1)

            def copy_h(t, j):
                act.wait_ge(h_summed, t + 1)
                nc.scalar.copy(h_rows[:, j % 2, :], ps_h[:, 0:A]).then_inc(h_rows_ready, 1)

            def relu(t, j, lang, fresh):
                act.wait_ge(h_turned, t + 1)
                if not (fresh and j < H_SLOTS):
                    act.wait_ge(adapted, t - H_SLOTS + 1)
                if not (fresh and j < H_T_SLOTS):
                    act.wait_ge(h_low_ready, t - H_T_SLOTS + 1)
                bias = b1_all[:, bass.ds(lang, 1)]
                nc.scalar.activation(h_high[:, j % H_SLOTS, :], ps_hT[:, 0:S], ACT.Relu, bias=bias).then_inc(h_high_ready, 1)
                nc.scalar.activation(h_T[:, j % H_T_SLOTS, :], ps_hT[:, 0:S], ACT.Relu, bias=bias).then_inc(h_T_ready, 1)

            def square(t, j):
                act.wait_ge(y_ready, t + 1)
                nc.scalar.activation(squares[:, j % 2, :], ps_y[j % Y_BANKS][:, :], ACT.Square, scale=-float(H),
                                     bias=row_sum[:, j:j + 1], accum_out=sq_sum[:, j:j + 1]).then_inc(squared, 1)

            def root(t, j):
                act.wait_ge(squared, t + 1)
                nc.scalar.activation(std[:, j - 1:j + 1], sq_sum[:, j - 1:j + 1], ACT.Sqrt, scale=float(H) ** -3,
                                     bias=eps[:, 0:1]).then_inc(std_ready, 1)

            def turn(i, first, last):
                behind = 0 if first else 1
                langs = first_langs if first else langs_of(act, i * UNROLL - behind, UNROLL - 1 + behind)
                for j in range(UNROLL):
                    t = i * UNROLL + j
                    if not (first and j == 0):
                        relu(t - 1, (j - 1) % UNROLL, langs[j - 1 + behind], first)
                    if not (last and j == UNROLL - 1):
                        copy_x_T(t + 1, (j + 1) % UNROLL, first and j < 1)
                    copy_h(t, j)
                    for u in seconds(j - 1, first, last):
                        norm_sums(i * UNROLL + u, u % UNROLL)

            def norm_sums(t, j):
                square(t, j)
                if j % 2 == 1:
                    root(t, j)

            act.wait_ge(s_b1, 16)
            copy_x_T(0, 0, True)
            all_turns(act, turn)
            relu(B - 1, UNROLL - 1, langs_of(act, B - 1, 1)[0], False)
            for k in range(LEFT_NORMS, 0, -1):
                norm_sums(B - k, UNROLL - k)

        @block.tensor
        def _(pe):
            def turn_x(t, i, j):
                if j % 2 == 0:
                    pe.wait_ge(x_loaded[j // 2], 16 * (i + 1))
                for c in range(C):
                    last = nc.tensor.transpose(ps_T[j % 2][:, c, :], x_io[:, j, c * 128:(c + 1) * 128], identity[:, :])
                last.then_inc(x_turned, 1)

            def first_product(t, j, lang):
                pe.wait_ge(x_T_ready, t + 1)
                for c in range(C):
                    last = nc.tensor.matmul(ps_h[:, 0:A], x_T[:, j % 2, c, :],
                                            w1_all[:, bass.ds(lang, 1), c, :].rearrange("p o a -> p (o a)"),
                                            start=(c == 0), stop=(c == C - 1))
                last.then_inc(h_summed, 1)

            def turn_h(t, j):
                pe.wait_ge(h_rows_ready, t + 1)
                nc.tensor.transpose(ps_hT[:, 0:S], h_rows[:, j % 2, :], identity[:, :]).then_inc(h_turned, 1)

            def second_product(t, j, lang, fresh, early):
                h = j % H_SLOTS
                if not fresh:
                    pe.wait_ge(out_ready, t - Y_BANKS + 1)
                bank = ps_y[j % Y_BANKS][:, :]
                with_b2 = not b2_by_pool(j, early)
                if with_b2:
                    nc.tensor.matmul(bank, of_lang(pick, lang), parts[:, :], start=True, stop=False)
                pe.wait_ge(h_high_ready, t + 1)
                nc.tensor.matmul(bank, h_high[:, h, :], of_lang(w2_high, lang), start=not with_b2, stop=False)
                nc.tensor.matmul(bank, h_high[:, h, :], of_lang(w2_low, lang), start=False, stop=False)
                pe.wait_ge(h_low_ready, t + 1)
                nc.tensor.matmul(bank, h_low[:, h, :], of_lang(w2_high, lang), start=False, stop=True)\
                    .then_inc(adapted, 1)

            def turn(i, first, last):
                behind = 0 if first else LAG
                langs = first_langs if first else langs_of(pe, i * UNROLL - behind, UNROLL + behind)
                for j in range(UNROLL):
                    t = i * UNROLL + j
                    early = first and j <= LAG
                    if not early:
                        turn_h(t - 1, (j - 1) % UNROLL)
                    if not (last and j == UNROLL - 1):
                        turn_x(t + 1, i + (j + 1) // UNROLL, (j + 1) % UNROLL)
                    if early and j > 0:
                        turn_h(t - 1, (j - 1) % UNROLL)
                    first_product(t, j, langs[j + behind])
                    if first and j == LAG:
                        pe.wait_ge(pick_ready, 3)
                        pe.wait_ge(spread_act, L)
                        pe.wait_ge(spread_dve, L)
                        pe.wait_ge(w2_low_ready, W_CHUNKS)
                    for u in seconds(j, first, last):
                        second_product(i * UNROLL + u, u % UNROLL, langs[u + behind], first and u < Y_BANKS, first)

            pe.wait_ge(identity_ready, 1)
            turn_x(0, 0, 0)
            pe.wait_ge(ids_ready, 1)
            first_langs = langs_of(pe, 0, UNROLL)
            pe.wait_ge(parts_ready, 48)
            pe.wait_ge(pick_ready, 1)
            for n in range(2 * L):
                if n == L:
                    pe.wait_ge(pick_ready, 2)
                if n >= Y_BANKS:
                    pe.wait_ge(spread_dve if n % 2 else spread_act, (n - Y_BANKS) // 2 + 1)
                nc.tensor.matmul(ps_y[n % Y_BANKS][:, :], pick[:, L + n, :], parts[:, :], start=True, stop=True)\
                    .then_inc(spread, 1)
            pe.wait_ge(s_w1, 16 * W_CHUNKS)
            all_turns(pe, turn)
            turn_h(B - 1, UNROLL - 1)
            langs = langs_of(pe, B - LEFT, LEFT)
            for k in range(LEFT, 0, -1):
                second_product(B - k, UNROLL - k, langs[LEFT - k], False, False)

        @block.vector
        def _(dve):
            dve.wait_ge(s_ids, 16)
            nc.vector.tensor_scalar(ids_fix[:, 0, :], ids_raw[:, :], 0.0, float(L), ALU.is_lt, ALU.mult).then_inc(ids_step, 1)
            dve.wait_ge(ids_step, 1)
            nc.vector.tensor_tensor(ids_fix[:, 1, :], ids_raw[:, :], ids_fix[:, 0, :], ALU.add).then_inc(ids_step, 1)
            dve.wait_ge(ids_step, 2)
            nc.vector.tensor_scalar(lang_ids[:, :], ids_fix[:, 1, :], 0.0, float(L - 1), ALU.max, ALU.min).then_inc(ids_ready, 1)
            dve.wait_ge(s_rows, 3 * 16)
            nc.vector.tensor_copy(cut[0:3 * L, 0, :], rows[:, :]).then_inc(cut_step, 1)
            dve.wait_ge(cut_step, 1)
            nc.vector.tensor_tensor(rows[:, :], rows[:, :], cut[0:3 * L, 0, :], ALU.subtract).then_inc(cut_step, 1)
            dve.wait_ge(cut_step, 2)
            nc.vector.tensor_copy(cut[0:3 * L, 1, :], rows[:, :]).then_inc(cut_step, 1)
            dve.wait_ge(cut_step, 3)
            nc.vector.tensor_tensor(rows[:, :], rows[:, :], cut[0:3 * L, 1, :], ALU.subtract).then_inc(cut_step, 1)
            dve.wait_ge(cut_step, 4)
            nc.vector.tensor_copy(cut[0:3 * L, 2, :], rows[:, :]).then_inc(cut_step, 1)
            for n in range(1, 2 * L, 2):
                dve.wait_ge(spread, n + 1)
                nc.vector.tensor_copy(spread_to(n), ps_y[n % Y_BANKS][:, :]).then_inc(spread_dve, 1)
            dve.wait_ge(spread_act, L)
            dve.wait_ge(spread_dve, L)
            for n in range(W_CHUNKS):
                dve.wait_ge(s_w2[n], 16)
                nc.vector.tensor_copy(w2_chunk(w2_high, n), w2_chunk(w2_all, n)).then_inc(w2_high_ready, 1)
                dve.wait_ge(w2_high_ready, n + 1)
                nc.vector.tensor_tensor(w2_chunk(w2_low, n), w2_chunk(w2_all, n), w2_chunk(w2_high, n).bitcast(F32),
                                        ALU.subtract).then_inc(w2_low_ready, 1)
            dve.wait_ge(ids_ready, 1)

            def add_x(t, i, j, early):
                dve.wait_ge(adapted, t + 1)
                x_rows = x_io[:, j, :]
                if b2_by_pool(j, early):
                    dve.wait_ge(x_b2_ready, b2_count(i, j))
                    x_rows = x_b2[:, b2_slot(j), :]
                bank = ps_y[j % Y_BANKS][:, :]
                nc.vector.scalar_tensor_tensor(bank, bank, 1.0, x_rows, ALU.mult, ALU.add,
                                               accum_out=row_sum[:, j:j + 1]).then_inc(y_ready, 1)

            def means(t, j):
                dve.wait_ge(y_ready, t + 1)
                nc.vector.tensor_scalar(mean[:, j - 1:j + 1], row_sum[:, j - 1:j + 1], 1.0 / H, None, ALU.mult)\
                    .then_inc(mean_ready, 1)

            def invert(q, j):
                dve.wait_ge(std_ready, q + 1)
                nc.vector.reciprocal(rstd[:, j:j + 2], std[:, j:j + 2]).then_inc(rstd_ready, 1)

            def scale(t, q, j, lang):
                if j % 2 == 0:
                    dve.wait_ge(mean_ready, q + 1)
                dve.wait_ge(squared, t + 1)
                bank = ps_y[j % Y_BANKS][:, :]
                nc.vector.scalar_tensor_tensor(bank, bank, mean[:, j:j + 1], of_lang(gamma_all, lang),
                                               ALU.subtract, ALU.mult).then_inc(scaled, 1)

            def finish(t, q, j):
                if j % 2 == 0:
                    dve.wait_ge(rstd_ready, q + 1)
                dve.wait_ge(scaled, t + 1)
                dve.wait_ge(x_beta_ready, t + 1)
                nc.vector.scalar_tensor_tensor(x_io[:, j, :], ps_y[j % Y_BANKS][:, :], rstd[:, j:j + 1],
                                               x_io[:, j, :], ALU.mult, ALU.add).then_inc(out_ready, 1)

            def step(i, j, langs, has_norm, has_means, has_sum, early=False):
                t = i * UNROLL + j
                late = (j - NORM_LAG) % UNROLL
                q = (i + (j - NORM_LAG) // UNROLL) * PAIRS + late // 2
                if has_norm:
                    if late % 2 == 0:
                        last_pair = not has_means and late == UNROLL - 2
                        if not last_pair:
                            invert(q, late)
                        for b in range(2):
                            scale(t - NORM_LAG + b, q, late + b, langs[b])
                        if last_pair:
                            invert(q, late)
                    finish(t - NORM_LAG, q, late)
                if has_means and j % 2 == 1:
                    means(t - 2, (j - 2) % UNROLL)
                if has_sum:
                    add_x(t - 1, i + (j - 1) // UNROLL, (j - 1) % UNROLL, early)

            def turn(i, first, last):
                behind = 0 if first else NORM_LAG
                langs = langs_of(dve, i * UNROLL - behind, UNROLL - NORM_LAG + behind)
                for j in range(UNROLL):
                    has_norm = not (first and j < NORM_LAG)
                    step(i, j, langs[j - NORM_LAG + behind:] if has_norm else None, has_norm,
                         not (first and j < 2), not (first and j == 0), first)

            all_turns(dve, turn)
            langs = langs_of(dve, B - NORM_LAG, NORM_LAG)
            for j in range(NORM_LAG):
                step(TURNS, j, langs[j:], True, j == 1, j == 0)


INPUTS = ["x", "itok_B_0_8", "L0_cond_W1", "L0_cond_b1", "L0_cond_W2", "L0_cond_b2", "L0_cond_gamma", "L0_cond_beta"]


def kernel(**inputs):
    import numpy as np
    import concourse.bacc as bacc
    from concourse.bass_utils import run_bass_kernel_spmd

    nc = bacc.Bacc("TRN2", target_bir_lowering=False, num_devices=1)
    arrays, args = {}, []
    for name in INPUTS:
        a = np.ascontiguousarray(inputs[name])
        arrays[f"in_{name}"] = a
        args.append(nc.dram_tensor(f"in_{name}", a.shape, mybir.dt.from_np(a.dtype), kind="ExternalInput").ap())
    out = nc.dram_tensor("out", inputs["x"].shape, F32, kind="ExternalOutput").ap()
    build(nc, *args, out)
    return run_bass_kernel_spmd(nc, [arrays], core_ids=[0]).results[0]["out"]
```
